# Optimizing a Trainium2 kernel written in Bass

```python
import numpy as np
import jax
import jax.numpy as jnp

def _softmax(x, axis=-1):
    return jax.nn.softmax(x, axis=axis)

def _gelu(x):
    return jax.nn.gelu(x, approximate=True)

def _silu(x):
    return jax.nn.silu(x)

def _sigmoid(x):
    return jax.nn.sigmoid(x)

def _layernorm(x, axis=-1, eps=1e-05):
    m = jnp.mean(x, axis=axis, keepdims=True)
    v = jnp.var(x, axis=axis, keepdims=True)
    return (x - m) / jnp.sqrt(v + eps)

def _scatter_add(tgt, idx, src, axis=0):
    return tgt.at[idx].add(src)

def _segment_sum(src, seg, n):
    return jax.ops.segment_sum(src, seg, n)
kernel_name = 'mk_adaln_ffn_d1_seqx_r4_418668'

def setup_inputs(seed: int=0):
    np.random.seed(seed)
    _w = jnp.asarray

    def _rec_inputs():
        import jax
        import jax.numpy as jnp
        _rk = jax.random.key(seed)
        x = -0.000125 + 0.9999 * jax.random.normal(jax.random.fold_in(_rk, 1), (32, 64, 1024), jnp.float32)
        _lenS = 64 - jax.random.randint(jax.random.fold_in(_rk, 7), (32,), 0, max(1, 64 // 4) + 1, jnp.int32)
        _lenS2 = 64 - jax.random.randint(jax.random.fold_in(_rk, 8), (32,), 0, max(1, 64 // 4) + 1, jnp.int32)
        itok_B_0_7 = jax.random.randint(jax.random.fold_in(_rk, 11), (32,), 0, 8, jnp.int32)
        return (x, itok_B_0_7)
    x, itok_B_0_7 = _rec_inputs()

    def _L0_cond_setup():
        import jax, jax.numpy as jnp
        import numpy as np
        TOP_K = 2
        LANG_BIAS = 5.0
        SCALING = 32.0 / 16.0
        LANGUAGE_PAD_ID = -1
        key = jax.random.key(seed)
        ks = jax.random.split(key, 6)
        B, T, D, O, E, R = (4, 512, 1024, 1024, 8, 16)
        x = jax.random.normal(ks[0], (B, T, D), dtype=jnp.float32)
        language_ids = jax.random.randint(ks[1], (B,), 0, E).astype(jnp.int64)
        W = jax.random.normal(ks[2], (O, D), dtype=jnp.float32) * (1.0 / np.sqrt(D))
        Wr = jax.random.normal(ks[3], (E, D), dtype=jnp.float32) * (1.0 / np.sqrt(D))
        A = jax.random.normal(ks[4], (E, R, D), dtype=jnp.float32) * (1.0 / np.sqrt(D))
        Bm = jax.random.normal(ks[5], (O, R), dtype=jnp.float32) * 0.0
        Bm = jnp.broadcast_to(Bm, (E, O, R)) + jax.random.normal(ks[5], (E, O, R), dtype=jnp.float32) * 0.02
        return {'x': x, 'language_ids': language_ids, 'W': W, 'Wr': Wr, 'A': A, 'B': Bm}
    _L0_cond_all = _L0_cond_setup()
    _L0_cond_in = {k: v for k, v in _L0_cond_all.items() if k in ('W', 'Wr', 'A', 'B')}
    del _L0_cond_all

    def _L0_ffn_setup():
        import jax, jax.numpy as jnp
        import numpy as np
        SCALE = 16.0 / 8.0
        key = jax.random.key(seed)
        ks = jax.random.split(key, 6)
        B, S, IN, OUT, E, R = (4, 512, 1024, 1024, 4, 8)
        x = jax.random.normal(ks[0], (B, S, IN), dtype=jnp.float32)
        W = jax.random.normal(ks[1], (OUT, IN), dtype=jnp.float32) * 0.02
        b = jax.random.normal(ks[2], (OUT,), dtype=jnp.float32) * 0.02
        A = jax.random.normal(ks[3], (E, R, IN), dtype=jnp.float32) * 0.02
        Bm = jax.random.normal(ks[4], (E, OUT, R), dtype=jnp.float32) * 0.02
        Wr = jax.random.normal(ks[5], (E, IN), dtype=jnp.float32) * 0.02
        return {'x': x, 'W': W, 'b': b, 'A': A, 'Bm': Bm, 'Wr': Wr}
    _L0_ffn_all = _L0_ffn_setup()
    _L0_ffn_in = {k: v for k, v in _L0_ffn_all.items() if k in ('W', 'b', 'A', 'Bm', 'Wr')}
    del _L0_ffn_all
    return {'x': x, 'itok_B_0_7': itok_B_0_7, 'L0_cond_W': _L0_cond_in['W'], 'L0_cond_Wr': _L0_cond_in['Wr'], 'L0_cond_A': _L0_cond_in['A'], 'L0_cond_B': _L0_cond_in['B'], 'L0_ffn_W': _L0_ffn_in['W'], 'L0_ffn_b': _L0_ffn_in['b'], 'L0_ffn_A': _L0_ffn_in['A'], 'L0_ffn_Bm': _L0_ffn_in['Bm'], 'L0_ffn_Wr': _L0_ffn_in['Wr']}

def reference(x, itok_B_0_7, L0_cond_W, L0_cond_Wr, L0_cond_A, L0_cond_B, L0_ffn_W, L0_ffn_b, L0_ffn_A, L0_ffn_Bm, L0_ffn_Wr):
    import jax
    import jax.numpy as jnp

    def _L0_cond_ref(x, language_ids, W, Wr, A, B):
        import jax, jax.numpy as jnp
        import numpy as np
        TOP_K = 2
        LANG_BIAS = 5.0
        SCALING = 32.0 / 16.0
        LANGUAGE_PAD_ID = -1
        base = jnp.einsum('btd,od->bto', x, W)
        E = Wr.shape[0]
        logits = jnp.einsum('btd,ed->bte', x.astype(jnp.float32), Wr.astype(jnp.float32))
        expert_targets = language_ids
        valid = expert_targets >= 0
        tgt = jnp.where(valid, expert_targets, 0)
        bias = jax.nn.one_hot(tgt, E, dtype=logits.dtype) * LANG_BIAS
        bias = jnp.where(valid[:, None], bias, 0.0)
        logits = logits + bias[:, None, :]
        topw, topi = jax.lax.top_k(logits, TOP_K)
        weights = jax.nn.softmax(topw, axis=-1)
        gates = jnp.sum(jax.nn.one_hot(topi, E, dtype=weights.dtype) * weights[..., None], axis=-2)
        gates = gates.astype(x.dtype)
        h = jnp.einsum('btd,erd->bter', x, A)
        lora_out = jnp.einsum('bter,bte,eor->bto', h, gates, B)
        return base + SCALING * lora_out

    def _L0_ffn_ref(x, W, b, A, Bm, Wr):
        import jax, jax.numpy as jnp
        import numpy as np
        SCALE = 16.0 / 8.0
        base_out = jnp.einsum('bsi,oi->bso', x, W) + b
        gates = jax.nn.softmax(jnp.einsum('bsi,ei->bse', x, Wr), axis=-1)
        proj_r = jnp.einsum('bsi,eri->bser', x, A)
        lora_out = jnp.einsum('bser,eor->bseo', proj_r, Bm)
        lora_mix = jnp.einsum('bse,bseo->bso', gates * SCALE, lora_out)
        return base_out + lora_mix
    x = x + _L0_ffn_ref(_L0_cond_ref(x, itok_B_0_7, L0_cond_W, L0_cond_Wr, L0_cond_A, L0_cond_B), L0_ffn_W, L0_ffn_b, L0_ffn_A, L0_ffn_Bm, L0_ffn_Wr)
    return x

_drawn_inputs = setup_inputs


def setup_inputs(seed=0):
    import zlib

    import numpy as np

    out = dict(_drawn_inputs(seed))
    spreads = {}
    factors = {'L0_cond_Wr': 6.978, 'L0_ffn_b': 3.315, 'L0_ffn_Wr': 3.433}
    for name, (base, spread) in spreads.items():
        noise = np.random.default_rng([zlib.crc32(name.encode()), seed]).standard_normal(out[name].shape)
        drawn = base * np.exp(spread * noise) if base else spread * noise
        out[name] = jnp.asarray(drawn.astype(out[name].dtype))
    for name, factor in factors.items():
        out[name] = (out[name] * factor).astype(out[name].dtype)
    return out
```

```python
import concourse.bass as bass
from concourse import mybir
from contextlib import ExitStack



def adaln_ffn_kernel(nc, head, fold_tail, tokens, gate_proj, mix_rows, language, out):
    F32 = mybir.dt.float32
    F32R = mybir.dt.float32r
    I32 = mybir.dt.int32
    U32 = mybir.dt.uint32
    ALU = mybir.AluOpType
    ACT = mybir.ActivationFunctionType
    AX = mybir.AxisListType

    P = 128
    D = out.shape[1]
    KC = D // P
    TILES = out.shape[0] // P
    HALF = 512
    E1 = 8
    ER1 = gate_proj.shape[2] - E1
    R1 = ER1 // E1
    MCOLS = head.shape[2] - 3 * P
    SMALL2 = MCOLS - D
    E2 = 4
    ER2 = SMALL2 - E2
    R2 = ER2 // E2
    SMALL = SMALL2 + ER1 + E1
    COLS = D + SMALL
    MIX = mix_rows.shape[0]
    LANG_BIAS = 5.0
    HEAD_W = MCOLS + 3 * P
    HEAD_TILES = 3
    PAIRED = KC + 1 - HEAD_TILES
    PROJ_AT, LOGIT_AT = SMALL2, SMALL2 + ER1

    GATE_LOAD, MIX_LOAD, PAIR_LOAD = KC, KC + 1, KC + 2

    ctx = ExitStack()
    with ctx:
        def sb(name, shape, dt=F32):
            return ctx.enter_context(nc.sbuf_tensor(name, shape, dt))

        def sem(name):
            return ctx.enter_context(nc.semaphore(name))

        c_high = sb("c_high", [P, 1 + KC, COLS], F32R)
        c_low = sb("c_low", [P, 1 + KC, COLS], F32R)
        st_high = sb("st_high", [P, 4, KC, P], F32R)
        st_low = sb("st_low", [P, 4, KC, P], F32R)
        stage = sb("stage", [P, 2, HEAD_W])
        mix = sb("mix", [MIX, D], F32R)
        mix_is_low = sb("mix_is_low", [P, 1])
        mix_sign = sb("mix_sign", [P, 1])
        ident = sb("ident", [P, P])
        ident_r = sb("ident_r", [P, P], F32R)
        lang_i = sb("lang_i", [P, TILES], I32)
        lang_f = sb("lang_f", [P, TILES])
        expert_no = sb("expert_no", [P, E1])
        lang_bias = sb("lang_bias", [P, TILES, E1])
        logits = sb("logits", [P, E1])
        top = sb("top", [P, E1])
        top_at = sb("top_at", [P, E1], U32)
        top_at_f = sb("top_at_f", [P, 2])
        pair_exp = sb("pair_exp", [P, 1])
        pair_half = sb("pair_half", [P, 1])
        pair_scale = sb("pair_scale", [P, 1])
        gate_second = sb("gate_second", [P, E1])
        gates = sb("gates", [P, E1])
        u = sb("u", [P, ER1])
        ut_high = sb("ut_high", [P, P], F32R)
        ut_low = sb("ut_low", [P, P], F32R)
        neg_max = sb("neg_max", [P, 1])
        y_exp = sb("y_exp", [P, E2])
        y_sum = sb("y_sum", [P, 1])
        y_half = sb("y_half", [P, 1])
        y_scale = sb("y_scale", [P, 1])
        v = sb("v", [P, ER2])
        v_rows = sb("v_rows", [P, MIX])
        vt = sb("vt", [MIX, P], F32R)
        with nc.sbuf_tensor("m_high", [P, KC, MCOLS], F32R) as m_high, \
                nc.sbuf_tensor("m_low", [P, KC, MCOLS], F32R) as m_low:
            pass
        rows = sb("rows", [P, 2, D])

        wide = ctx.enter_context(nc.psum_tensor("wide", [P, 3, D], F32))
        narrow = ctx.enter_context(nc.psum_tensor("narrow", [P, 2, HALF], F32))
        ut_psum = wide[:, 2, 0:P]
        vt_psum = wide[0:MIX, 2, HALF:HALF + P]

        staged = [sem("staged_0"), sem("staged_1")]
        lang_here = sem("lang_here")
        ident_zero = sem("ident_zero")
        ident_made = sem("ident_made")
        ident_rounded = sem("ident_rounded")
        mask_zero = sem("mask_zero")
        mask_made = sem("mask_made")
        mask_sign = sem("mask_sign")
        expert_made = sem("expert_made")
        high_made = sem("high_made")
        low_made = sem("low_made")
        mix_tmp = sem("mix_tmp")
        contracted = sem("contracted")
        fold_high = sem("fold_high")
        banks_free = [sem("banks_free_0"), sem("banks_free_1"), sem("banks_free_2")]
        folded = sem("folded")
        vec = sem("vec")
        carried = sem("carried")
        top_ready = sem("top_ready")
        pair_exp_ready = sem("pair_exp_ready")
        u_ready = sem("u_ready")
        u_turned = sem("u_turned")
        ut_high_ready = sem("ut_high_ready")
        ut_low_ready = sem("ut_low_ready")
        y_small_ready = sem("y_small_ready")
        neg_max_ready = sem("neg_max_ready")
        y_exp_ready = sem("y_exp_ready")
        v_high_ready = sem("v_high_ready")
        v_ready = sem("v_ready")
        v_turned = sem("v_turned")
        vt_ready = sem("vt_ready")
        z_ready = sem("z_ready")
        left_ready = sem("left_ready")
        right_ready = sem("right_ready")
        rows_free = [sem("rows_free_0"), sem("rows_free_1")]

        def high_bits(t):
            return t.bitcast(F32)

        block = ctx.enter_context(nc.Block())

        SLOT = (3, 0)
        NARROW = (1, 0)
        JT = PAIRED // 2

        @block.sync
        def _(sp):
            def stage_is_free(n):
                sp.wait_ge(low_made, n - 1)

            def into_stage(par, src, width, rows_=P):
                sp.dma_start(stage[0:rows_, par, 0:width], src).then_inc(staged[par], 16)

            for k in range(KC):
                if k >= 2:
                    stage_is_free(k)
                into_stage(k % 2, head[k], HEAD_W)
            stage_is_free(GATE_LOAD)
            into_stage(GATE_LOAD % 2, gate_proj.rearrange("p k c -> p (k c)"), KC * (ER1 + E1))
            stage_is_free(MIX_LOAD)
            into_stage(MIX_LOAD % 2, mix_rows, D, MIX)
            for q in range(PAIRED):
                stage_is_free(PAIR_LOAD + q)
                into_stage(q % 2, fold_tail[q], D)
            for t in range(2):
                stage_is_free(PAIR_LOAD + PAIRED + t)
                into_stage(t, tokens[t], D)

            def store(j, par, t):
                sp.wait_ge(left_ready, t + 1)
                sp.wait_ge(right_ready, t + 1)
                sp.dma_start(out[bass.ds(t * P, P), :], rows[:, par, :]).then_inc(rows_free[par], 16)

            with sp.Fori(0, TILES // 2 - 1) as j:
                stage_is_free(PAIR_LOAD + PAIRED + 2 + 2 * j)
                into_stage(0, tokens[2 * j + 2], D)
                store(j, 0, 2 * j)
                stage_is_free(PAIR_LOAD + PAIRED + 3 + 2 * j)
                into_stage(1, tokens[2 * j + 3], D)
                store(j, 1, 2 * j + 1)
            store(TILES // 2 - 1, 0, TILES - 2)
            store(TILES // 2 - 1, 1, TILES - 1)
            sp.wait_ge(rows_free[0], 16 * (TILES // 2) + 1)
            sp.wait_ge(rows_free[1], 16 * (TILES // 2) + 1)

        @block.gpsimd
        def _(pool):
            nc.gpsimd.memset(ident[:, :], 0.0).then_inc(ident_zero, 1)
            pool.wait_ge(ident_zero, 1)
            nc.gpsimd.affine_select(out=ident[:, :], in_=ident[:, :], compare_op=ALU.not_equal, fill=1.0,
                                    base=0, pattern=[[-1, P]], channel_multiplier=1).then_inc(ident_made, 1)
            nc.gpsimd.iota(expert_no[:, :], pattern=[[1, E1]], base=0, channel_multiplier=0,
                           allow_small_or_imprecise_dtypes=True).then_inc(expert_made, 1)
            nc.gpsimd.memset(mix_is_low[:, :], 0.0).then_inc(mask_zero, 1)
            pool.wait_ge(mask_zero, 1)
            nc.gpsimd.memset(mix_is_low[ER2:2 * ER2, :], 1.0).then_inc(mask_zero, 1)
            pool.wait_ge(mask_zero, 2)
            nc.gpsimd.affine_select(out=mix_is_low[:, :], in_=mix_is_low[:, :], compare_op=ALU.not_equal, fill=1.0,
                                    base=-(MIX - 1), pattern=[[0, 1]], channel_multiplier=1).then_inc(mask_made, 1)
            pool.wait_ge(mask_made, 1)
            nc.gpsimd.tensor_scalar(mix_sign[:, :], mix_is_low[:, :], -2.0, 1.0, ALU.mult, ALU.add).then_inc(mask_sign, 1)

        @block.scalar
        def _(act):
            act.dma_start(lang_i[:, :], language).then_inc(lang_here, 16)

            def copy(out_, in_):
                return nc.scalar.activation(out_, in_, ACT.Copy)

            for k in range(KC):
                act.wait_ge(staged[k % 2], 16 * (k // 2 + 1))
                copy(st_high[:, 0:HEAD_TILES, k, :],
                     stage[:, k % 2, MCOLS:HEAD_W].rearrange("p (s c) -> p s c", c=P))
                copy(m_high[:, k, :], stage[:, k % 2, 0:MCOLS]).then_inc(high_made, 1)
            act.wait_ge(staged[GATE_LOAD % 2], 16 * (GATE_LOAD // 2 + 1))
            copy(c_high[:, 1:1 + KC, MCOLS:COLS],
                 stage[:, GATE_LOAD % 2, 0:KC * (ER1 + E1)].rearrange("p (k c) -> p k c", k=KC)).then_inc(high_made, 1)
            act.wait_ge(staged[MIX_LOAD % 2], 16 * (MIX_LOAD // 2 + 1))
            copy(mix[:, :], stage[0:MIX, MIX_LOAD % 2, 0:D]).then_inc(high_made, 1)

            def round_tile(j, par):
                act.wait_ge(staged[par], 16 * (PAIR_LOAD // 2 + 1) + 16 * j)
                copy(st_high[:, SLOT[par], :, :].rearrange("p k c -> p (k c)"),
                     stage[:, par, 0:D]).then_inc(high_made, 1)

            def fold_piece(dst, src):
                copy(dst, src).then_inc(fold_high, 1)

            round_tile(0, 0)
            for s in range(HEAD_TILES):
                act.wait_ge(contracted, s + 1)
                for h in range(2):
                    fold_piece(c_high[:, s, h * HALF:(h + 1) * HALF], wide[:, s, h * HALF:(h + 1) * HALF])
            fold_piece(c_high[:, 0:HEAD_TILES, D:MCOLS],
                       narrow[:, 0, 0:HEAD_TILES * SMALL2].rearrange("p (s c) -> p s c", c=SMALL2))

            def fold_out(j, par):
                s = 2 * j + par + HEAD_TILES
                act.wait_ge(contracted, s + 1)
                for h in range(2):
                    fold_piece(c_high[:, s, h * HALF:(h + 1) * HALF], wide[:, par, h * HALF:(h + 1) * HALF])
                fold_piece(c_high[:, s, D:MCOLS], narrow[:, NARROW[par], 0:SMALL2])

            with act.Fori(0, JT) as j:
                act.wait_ge(contracted, 2 * j + HEAD_TILES)
                round_tile(j, 1)
                fold_out(j, 0)
                round_tile(j + 1, 0)
                fold_out(j, 1)

            def next_tile(j, par):
                act.wait_ge(contracted, 2 * j + par + HEAD_TILES - 1)
                round_tile(j, par)

            def finish(t, j, par, with_next):
                act.wait_ge(top_ready, t + 1)
                nc.scalar.activation(pair_exp[:, :], top[:, 0:1], ACT.Exp, bias=top[:, 1:2],
                                     scale=-1.0).then_inc(pair_exp_ready, 1)
                if with_next:
                    next_tile(JT + j + 1, par)
                act.wait_ge(u_turned, t + 1)
                copy(ut_high[:, :], ut_psum).then_inc(ut_high_ready, 1)
                act.wait_ge(neg_max_ready, t + 1)
                nc.scalar.activation(y_exp[:, :], narrow[:, NARROW[par], 0:E2], ACT.Exp, bias=neg_max[:, 0:1],
                                     accum_out=y_sum[:, :]).then_inc(y_exp_ready, 1)
                act.wait_ge(v_turned, t + 1)
                copy(vt[:, :], vt_psum).then_inc(vt_ready, 1)
                act.wait_ge(z_ready, t + 1)
                act.wait_ge(rows_free[par], 16 * j + 1)
                copy(rows[:, par, 0:HALF], wide[:, par, 0:HALF])\
                    .then_inc(left_ready, 1)
                act.wait_ge(left_ready, t + 1)
                act.sem_inc(banks_free[par], 1)

            next_tile(JT, 1)
            with act.Fori(0, TILES // 2 - 1) as j:
                finish(2 * j, j, 0, True)
                finish(2 * j + 1, j, 1, True)
            finish(TILES - 2, TILES // 2 - 1, 0, False)
            finish(TILES - 1, TILES // 2 - 1, 1, False)

        @block.vector
        def _(dve):
            dve.wait_ge(ident_made, 1)
            nc.vector.tensor_copy(ident_r[:, :], ident[:, :]).then_inc(ident_rounded, 1)
            for par in range(2):
                nc.vector.memset(v_rows[:, 3 * ER2 + par:3 * ER2 + par + 1], 1.0).then_inc(rows_free[par], 1)

            def low_part(dst, src, high):
                return nc.vector.tensor_tensor(dst, src, high_bits(high), ALU.subtract)

            for k in range(KC):
                dve.wait_ge(high_made, k + 1)
                low_part(st_low[:, 0:HEAD_TILES, k, :],
                         stage[:, k % 2, MCOLS:HEAD_W].rearrange("p (s c) -> p s c", c=P),
                         st_high[:, 0:HEAD_TILES, k, :])
                low_part(m_low[:, k, :], stage[:, k % 2, 0:MCOLS], m_high[:, k, :]).then_inc(low_made, 1)
            dve.wait_ge(high_made, GATE_LOAD + 1)
            low_part(c_low[:, 1:1 + KC, MCOLS:COLS],
                     stage[:, GATE_LOAD % 2, 0:KC * (ER1 + E1)].rearrange("p (k c) -> p k c", k=KC),
                     c_high[:, 1:1 + KC, MCOLS:COLS]).then_inc(low_made, 1)
            dve.wait_ge(high_made, MIX_LOAD + 1)
            dve.wait_ge(mask_sign, 1)
            staged_mix = stage[0:MIX, MIX_LOAD % 2, 0:D]
            nc.vector.tensor_scalar(staged_mix, staged_mix, mix_is_low[0:MIX, 0:1], None, ALU.mult).then_inc(mix_tmp, 1)
            dve.wait_ge(mix_tmp, 1)
            nc.vector.scalar_tensor_tensor(out=mix[:, :], in0=high_bits(mix[:, :]), scalar=mix_sign[0:MIX, 0:1],
                                           in1=staged_mix, op0=ALU.mult, op1=ALU.add).then_inc(low_made, 1)

            dve.wait_ge(lang_here, 16)
            dve.wait_ge(expert_made, 1)
            nc.vector.tensor_copy(lang_f[:, :], lang_i[:, :]).then_inc(vec, 1)
            dve.wait_ge(vec, 1)
            nc.vector.tensor_tensor(lang_bias[:, :, :], lang_f[:, :].unsqueeze(2).to_broadcast([P, TILES, E1]),
                                    expert_no[:, :].unsqueeze(1).to_broadcast([P, TILES, E1]),
                                    ALU.is_equal).then_inc(vec, 1)
            dve.wait_ge(vec, 2)
            nc.vector.tensor_scalar(lang_bias[:, :, :], lang_bias[:, :, :], LANG_BIAS, None, ALU.mult).then_inc(vec, 1)
            VEC_START = 3

            def low_tile(j, par, n):
                dve.wait_ge(high_made, n + 1)
                low_part(st_low[:, SLOT[par], :, :].rearrange("p k c -> p (k c)"), stage[:, par, 0:D],
                         st_high[:, SLOT[par], :, :].rearrange("p k c -> p (k c)")).then_inc(low_made, 1)

            low_tile(0, 0, PAIR_LOAD)
            piece = 0
            for s in range(HEAD_TILES):
                for h in range(2):
                    piece += 1
                    dve.wait_ge(fold_high, piece)
                    last = low_part(c_low[:, s, h * HALF:(h + 1) * HALF], wide[:, s, h * HALF:(h + 1) * HALF],
                                    c_high[:, s, h * HALF:(h + 1) * HALF])
                if s < 2:
                    last.then_inc(banks_free[s], 1)
            piece += 1
            dve.wait_ge(fold_high, piece)
            low_part(c_low[:, 0:HEAD_TILES, D:MCOLS],
                     narrow[:, 0, 0:HEAD_TILES * SMALL2].rearrange("p (s c) -> p s c", c=SMALL2),
                     c_high[:, 0:HEAD_TILES, D:MCOLS]).then_inc(banks_free[2], 1)
            HEAD_PIECES = piece

            def fold_out(j, par):
                s = 2 * j + par + HEAD_TILES
                for h in range(2):
                    dve.wait_ge(fold_high, 6 * j + HEAD_PIECES + 3 * par + h + 1)
                    low_part(c_low[:, s, h * HALF:(h + 1) * HALF], wide[:, par, h * HALF:(h + 1) * HALF],
                             c_high[:, s, h * HALF:(h + 1) * HALF])
                dve.wait_ge(fold_high, 6 * j + HEAD_PIECES + 3 * par + 3)
                low_part(c_low[:, s, D:MCOLS], narrow[:, NARROW[par], 0:SMALL2],
                         c_high[:, s, D:MCOLS]).then_inc(banks_free[par], 1)

            with dve.Fori(0, JT) as j:
                low_tile(j, 1, 2 * j + PAIR_LOAD + 1)
                fold_out(j, 0)
                low_tile(j + 1, 0, 2 * j + PAIR_LOAD + 2)
                fold_out(j, 1)

            STEPS = 11

            def finish(t, j, par, with_next):
                nb = NARROW[par]
                base = STEPS * t + VEC_START
                step = [0]

                def link(ins):
                    step[0] += 1
                    ins.then_inc(vec, 1)
                    dve.wait_ge(vec, base + step[0])

                dve.wait_ge(contracted, t + KC + 2)
                link(nc.vector.tensor_tensor(logits[:, :], narrow[:, nb, LOGIT_AT:LOGIT_AT + E1],
                                             lang_bias[:, t, :], ALU.add))
                dve.sem_inc(carried, 1)
                link(nc.vector.max(top[:, :], logits[:, :]))
                dve.sem_inc(carried, 1)
                nc.vector.max_index(top_at[:, :], top[:, :], logits[:, :]).then_inc(top_ready, 1)
                dve.wait_ge(top_ready, t + 1)
                link(nc.vector.tensor_copy(top_at_f[:, :], top_at[:, 0:2]))
                dve.wait_ge(pair_exp_ready, t + 1)
                link(nc.vector.tensor_scalar(pair_half[:, :], pair_exp[:, :], 0.5, 0.5, ALU.mult, ALU.add))
                nc.vector.reciprocal(pair_scale[:, :], pair_half[:, :])
                link(nc.vector.tensor_scalar(gate_second[:, :], expert_no[:, :], top_at_f[:, 1:2], pair_exp[:, 0:1],
                                             ALU.is_equal, ALU.mult))
                link(nc.vector.scalar_tensor_tensor(out=gates[:, :], in0=expert_no[:, :], scalar=top_at_f[:, 0:1],
                                                    in1=gate_second[:, :], op0=ALU.is_equal, op1=ALU.add))
                nc.vector.scalar_tensor_tensor(
                    out=u[:, :].rearrange("p (e r) -> p e r", e=E1),
                    in0=narrow[:, nb, PROJ_AT:PROJ_AT + ER1].rearrange("p (e r) -> p e r", e=E1),
                    scalar=pair_scale[:, 0:1], in1=gates[:, :].unsqueeze(2).to_broadcast([P, E1, R1]),
                    op0=ALU.mult, op1=ALU.mult).then_inc(u_ready, 1)
                if with_next:
                    low_tile(j + 1, par, t + PAIR_LOAD + PAIRED + 2)
                dve.wait_ge(ut_high_ready, t + 1)
                low_part(ut_low[:, :], ut_psum, ut_high[:, :]).then_inc(ut_low_ready, 1)
                dve.wait_ge(y_small_ready, t + 1)
                nc.vector.tensor_reduce(neg_max[:, :], narrow[:, nb, 0:E2], AX.X, ALU.max,
                                        negate=True).then_inc(neg_max_ready, 1)
                dve.wait_ge(y_exp_ready, t + 1)
                link(nc.vector.tensor_scalar(y_half[:, :], y_sum[:, :], 0.5, None, ALU.mult))
                link(nc.vector.reciprocal(y_scale[:, :], y_half[:, :]))
                link(nc.vector.scalar_tensor_tensor(
                    out=v[:, :].rearrange("p (e r) -> p e r", e=E2),
                    in0=narrow[:, nb, E2:SMALL2].rearrange("p (e r) -> p e r", e=E2),
                    scalar=y_scale[:, 0:1], in1=y_exp[:, :].unsqueeze(2).to_broadcast([P, E2, R2]),
                    op0=ALU.mult, op1=ALU.mult))
                link(nc.vector.tensor_copy(
                    v_rows[:, 0:2 * ER2].bitcast(F32R).rearrange("p (a c) -> p a c", a=2),
                    v[:, :].unsqueeze(1).to_broadcast([P, 2, ER2])))
                link(nc.vector.tensor_tensor(v_rows[:, 2 * ER2:3 * ER2], v[:, :], v_rows[:, 0:ER2], ALU.subtract))
                assert step[0] == STEPS, step
                dve.sem_inc(v_ready, 1)
                dve.wait_ge(z_ready, t + 1)
                dve.wait_ge(rows_free[par], 16 * j + 1)
                nc.vector.tensor_copy(rows[:, par, HALF:D], wide[:, par, HALF:D]).then_inc(right_ready, 1)
                dve.wait_ge(right_ready, t + 1)
                dve.sem_inc(banks_free[par], 1)

            low_tile(0, 1, PAIR_LOAD + PAIRED + 1)
            with dve.Fori(0, TILES // 2 - 1) as j:
                finish(2 * j, j, 0, True)
                finish(2 * j + 1, j, 1, True)
            finish(TILES - 2, TILES // 2 - 1, 0, False)
            finish(TILES - 1, TILES // 2 - 1, 1, False)

        @block.tensor
        def _(pe):
            def mm(out_, lhs, rhs, start=False, stop=False):
                return nc.tensor.matmul(out_, lhs, rhs, start=start, stop=stop, skip_group_check=True)

            def products(slot, k, banks, cols, high, low, narrow_start):
                for lhs, rhs, first in ((st_high, high, True), (st_high, low, False), (st_low, high, False)):
                    for dst, a, b in ((banks[0], 0, HALF), (banks[1], HALF, D), (banks[2], D, cols)):
                        opens = k == 0 and first and (narrow_start or a < D)
                        last = mm(dst, lhs[:, slot, k, :], rhs[:, a:b], start=opens,
                                  stop=k == KC - 1 and lhs is st_low)
                return last

            pe.wait_ge(ident_rounded, 1)
            for k in range(KC):
                pe.wait_ge(low_made, k + 1)
                for s in range(HEAD_TILES):
                    last = products(s, k, (wide[:, s, 0:HALF], wide[:, s, HALF:D],
                                           narrow[:, 0, s * SMALL2:(s + 1) * SMALL2]),
                                    MCOLS, m_high[:, k, :], m_low[:, k, :], s == 0)
                    if k == KC - 1:
                        if s > 0:
                            last = mm(wide[:, s, (s - 1) * P:s * P], ident_r[:, :], ident_r[:, :])
                        last.then_inc(contracted, 1)

            pe.wait_ge(banks_free[2], 1)

            def fold_tile(j, par):
                pe.wait_ge(low_made, 2 * j + PAIR_LOAD + par + 1)
                pe.wait_ge(banks_free[par], j + 1)
                for k in range(KC):
                    products(SLOT[par], k, (wide[:, par, 0:HALF], wide[:, par, HALF:D],
                                            narrow[:, NARROW[par], 0:SMALL2]),
                             MCOLS, m_high[:, k, :], m_low[:, k, :], True)
                d = 2 * j + par + HEAD_TILES - 1
                mm(wide[:, par, bass.ds(d * P, P)], ident_r[:, :], ident_r[:, :]).then_inc(contracted, 1)

            with pe.Fori(0, JT) as j:
                fold_tile(j, 0)
                fold_tile(j, 1)

            def contract(t, j, par, between):
                pe.wait_ge(low_made, t + PAIR_LOAD + PAIRED + 1)
                pe.wait_ge(banks_free[par], 2 * j + JT + 1)
                for k in range(KC):
                    last = products(SLOT[par], k, (wide[:, par, 0:HALF], wide[:, par, HALF:D],
                                                   narrow[:, NARROW[par], 0:SMALL]),
                                    COLS, c_high[:, 1 + k, :], c_low[:, 1 + k, :], True)
                    if k == KC - 1:
                        last.then_inc(contracted, 1)
                    if k in between:
                        between[k]()

            def turn_u(t, par):
                pe.wait_ge(u_ready, t + 1)
                nc.tensor.transpose(ut_psum, u[:, :], ident[:, :]).then_inc(u_turned, 1)

            def lora_u(t, par):
                pe.wait_ge(ut_high_ready, t + 1)
                pe.wait_ge(ut_low_ready, t + 1)
                parts = ((ut_high, c_high), (ut_high, c_low), (ut_low, c_high))
                for lhs, rhs in parts:
                    last = mm(narrow[:, NARROW[par], 0:SMALL2], lhs[:, :], rhs[:, 0, D:MCOLS])
                last.then_inc(y_small_ready, 1)
                for lhs, rhs in parts:
                    for h in range(2):
                        mm(wide[:, par, h * HALF:(h + 1) * HALF], lhs[:, :], rhs[:, 0, h * HALF:(h + 1) * HALF])

            def turn_v(t, par):
                pe.wait_ge(v_ready, t + 1)
                nc.tensor.transpose(vt_psum, v_rows[:, :], ident[:, :]).then_inc(v_turned, 1)

            def lora_v(t, par):
                pe.wait_ge(vt_ready, t + 1)
                for h in range(2):
                    last = mm(wide[:, par, h * HALF:(h + 1) * HALF], vt[:, :], mix[:, h * HALF:(h + 1) * HALF])
                last.then_inc(z_ready, 1)

            def finishing(t, par):
                return {1: lambda: turn_u(t, par), 3: lambda: lora_u(t, par),
                        5: lambda: turn_v(t, par), 6: lambda: lora_v(t, par)}

            contract(0, 0, 0, {KC - 2: lambda: pe.wait_ge(banks_free[1], JT + 1)})
            with pe.Fori(0, TILES // 2 - 1) as j:
                contract(2 * j + 1, j, 1, finishing(2 * j, 0))
                contract(2 * j + 2, j + 1, 0, finishing(2 * j + 1, 1))
            contract(TILES - 1, TILES // 2 - 1, 1, finishing(TILES - 2, 0))
            for part in finishing(TILES - 1, 1).values():
                part()


def kernel(**inputs):
    import numpy as np
    import concourse.bacc as bacc
    from concourse.bass_utils import run_bass_kernel_spmd

    P = 128
    x = np.asarray(inputs["x"])
    batch, seq, D = x.shape
    KC = D // P
    tokens = batch * seq
    tiles = tokens // P
    W, Wr, A, B = (np.asarray(inputs["L0_cond_" + n]) for n in ("W", "Wr", "A", "B"))
    Wf, bf, Af, Bm, Wrf = (np.asarray(inputs["L0_ffn_" + n]) for n in ("W", "b", "A", "Bm", "Wr"))

    m_t = np.concatenate([Wf, Wrf, Af.reshape(-1, D)], axis=0).T
    b_t = B.transpose(1, 0, 2).reshape(D, -1)
    head = np.concatenate([m_t, b_t, W[:, :2 * P]], axis=1).reshape(KC, P, -1)
    fold_tail = W[:, 2 * P:].reshape(KC, P, KC - 2, P).transpose(2, 1, 0, 3).reshape(KC - 2, P, D)
    x_t = x.reshape(tiles, P, KC, P).transpose(0, 3, 2, 1).reshape(tiles, P, D)
    gate_proj = np.concatenate([A.reshape(-1, D), Wr], axis=0).T.reshape(KC, P, -1).transpose(1, 0, 2)
    bm_t = Bm.transpose(0, 2, 1).reshape(-1, D)
    mix_rows = np.concatenate([bm_t, bm_t, bm_t, bf[None], bf[None]], axis=0)
    language = np.repeat(np.asarray(inputs["itok_B_0_7"]), seq).reshape(tiles, P).T

    arrays = dict(head=head, fold_tail=fold_tail, tokens=x_t, gate_proj=gate_proj, mix_rows=mix_rows,
                  language=language)
    arrays = {n: np.ascontiguousarray(a) for n, a in arrays.items()}
    nc = bacc.Bacc("TRN2", target_bir_lowering=False, num_devices=1)
    args = [nc.dram_tensor(n, a.shape, mybir.dt.from_np(a.dtype), kind="ExternalInput").ap()
            for n, a in arrays.items()]
    out = nc.dram_tensor("out", (tokens, D), mybir.dt.float32, kind="ExternalOutput").ap()
    adaln_ffn_kernel(nc, *args, out)
    r = run_bass_kernel_spmd(nc, [arrays], core_ids=[0])
    return r.results[0]["out"].reshape(batch, seq, D)
```

```python
import concourse.bass as bass
from concourse import mybir
from contextlib import ExitStack



def adaln_ffn_kernel(nc, head, fold_tail, tokens, gate_proj, mix_rows, language, out):
    F32 = mybir.dt.float32
    F32R = mybir.dt.float32r
    I32 = mybir.dt.int32
    U32 = mybir.dt.uint32
    ALU = mybir.AluOpType
    ACT = mybir.ActivationFunctionType
    AX = mybir.AxisListType

    P = 128
    BANK = 512
    D = out.shape[1]
    KC = D // P
    TILES = out.shape[0] // P
    HEAD_TILES = 2
    HEAD_W = head.shape[2]
    MCOLS = HEAD_W - HEAD_TILES * P
    E1 = 8
    ER1 = gate_proj.shape[2] - E1
    R1 = ER1 // E1
    E2 = 4
    SMALL2 = MCOLS - D
    ER2 = SMALL2 - E2
    R2 = ER2 // E2
    COLS = MCOLS + ER1 + E1
    MIX = mix_rows.shape[0]
    LANG_BIAS = 5.0

    FOLD_CUT = (0, 3 * P, 6 * P, MCOLS)
    N_TAIL = 2 * P
    WIDE = (COLS - N_TAIL) // 2
    TOKEN_CUT = (0, WIDE, 2 * WIDE, COLS)
    Z_TAIL = D - 2 * WIDE
    LOGIT2_AT = Z_TAIL
    PROJ2_AT = LOGIT2_AT + E2
    PROJ_AT = Z_TAIL + SMALL2
    LOGIT_AT = PROJ_AT + ER1
    ORDER = (2, 0, 1)

    HEAD_BUFS = 3
    GATE_LOAD, MIX_LOAD, PAIR_LOAD = KC, KC + 1, KC + 2
    PAIR_STAGED = (KC + 2) // 3 + 1
    FOLDS = KC + 1 - HEAD_TILES
    SLOT = (2, 0)
    FOLD_PIECES = (3 * (1 + (FOLDS + 1) // 2), 3 * (1 + FOLDS // 2))

    ctx = ExitStack()
    with ctx:
        def sb(name, shape, dt=F32):
            return ctx.enter_context(nc.sbuf_tensor(name, shape, dt))

        def sem(name):
            return ctx.enter_context(nc.semaphore(name))

        c_high = sb("c_high", [P, 1 + KC, COLS], F32R)
        c_low = sb("c_low", [P, 1 + KC, COLS], F32R)
        st_high = sb("st_high", [P, 3, KC, P], F32R)
        st_low = sb("st_low", [P, 3, KC, P], F32R)
        stage = sb("stage", [P, HEAD_BUFS, HEAD_W])
        mix = sb("mix", [MIX, D], F32R)
        mix_is_low = sb("mix_is_low", [P, 1])
        mix_sign = sb("mix_sign", [P, 1])
        ident = sb("ident", [P, P])
        ident_r = sb("ident_r", [P, P], F32R)
        lang_i = sb("lang_i", [P, TILES], I32)
        lang_f = sb("lang_f", [P, TILES])
        expert_no = sb("expert_no", [P, E1])
        lang_bias = sb("lang_bias", [P, TILES, E1])
        logits = sb("logits", [P, E1])
        top = sb("top", [P, E1])
        top_at = sb("top_at", [P, E1], U32)
        top_at_f = sb("top_at_f", [P, 2])
        pair_exp = sb("pair_exp", [P, 1])
        pair_half = sb("pair_half", [P, 1])
        pair_scale = sb("pair_scale", [P, 1])
        gate_second = sb("gate_second", [P, E1])
        gates = sb("gates", [P, E1])
        u = sb("u", [P, ER1])
        ut_high = sb("ut_high", [P, P], F32R)
        ut_low = sb("ut_low", [P, P], F32R)
        neg_max = sb("neg_max", [P, 1])
        y_exp = sb("y_exp", [P, E2])
        y_sum = sb("y_sum", [P, 1])
        y_half = sb("y_half", [P, 1])
        y_scale = sb("y_scale", [P, 1])
        v = sb("v", [P, ER2])
        v_rows = sb("v_rows", [P, MIX])
        vt = sb("vt", [MIX, P], F32R)
        with nc.sbuf_tensor("m_high", [P, KC, MCOLS], F32R) as m_high, \
                nc.sbuf_tensor("m_low", [P, KC, MCOLS], F32R) as m_low:
            pass
        rows = sb("rows", [P, 2, D])

        sums = ctx.enter_context(nc.psum_tensor("sums", [P, 6, BANK], F32))
        turned = ctx.enter_context(nc.psum_tensor("turned", [P, 2, BANK], F32))
        ut_psum = turned[:, 0, 0:P]
        vt_psum = turned[0:MIX, 1, 0:P]

        staged = [sem(f"staged_{i}") for i in range(HEAD_BUFS)]
        lang_here = sem("lang_here")
        ident_zero = sem("ident_zero")
        ident_made = sem("ident_made")
        ident_rounded = sem("ident_rounded")
        mask_zero = sem("mask_zero")
        mask_made = sem("mask_made")
        mask_sign = sem("mask_sign")
        expert_made = sem("expert_made")
        high_made = sem("high_made")
        low_made = sem("low_made")
        mix_masked = sem("mix_masked")
        contracted = sem("contracted")
        fold_high = sem("fold_high")
        read_out = [sem("read_out_0"), sem("read_out_1")]
        vec = sem("vec")
        carried = sem("carried")
        narrow_ready = sem("narrow_ready")
        top_ready = sem("top_ready")
        pair_exp_ready = sem("pair_exp_ready")
        u_ready = sem("u_ready")
        u_turned = sem("u_turned")
        ut_high_ready = sem("ut_high_ready")
        ut_low_ready = sem("ut_low_ready")
        y_small_ready = sem("y_small_ready")
        neg_max_ready = sem("neg_max_ready")
        y_exp_ready = sem("y_exp_ready")
        v_ready = sem("v_ready")
        v_turned = sem("v_turned")
        vt_ready = sem("vt_ready")
        z_ready = sem("z_ready")
        rows_free = [sem("rows_free_0"), sem("rows_free_1")]

        def as_f32(t):
            return t.bitcast(F32)

        def piece(par, p, a=0, b=BANK):
            return sums[:, 3 * par + p, a:b]

        TPAR = (1, 0)
        TPAIR = (FOLDS // 2, (FOLDS + 1) // 2)

        block = ctx.enter_context(nc.Block())

        @block.sync
        def _(sp):
            def into_stage(buf, src, width, part=P):
                sp.dma_start(stage[0:part, buf, 0:width], src).then_inc(staged[buf], 16)

            for k in range(KC):
                if k >= HEAD_BUFS:
                    sp.wait_ge(low_made, k - HEAD_BUFS + 1)
                into_stage(k % HEAD_BUFS, head[k], HEAD_W)
            sp.wait_ge(low_made, GATE_LOAD - 1)
            into_stage(0, gate_proj.rearrange("p k c -> p (k c)"), KC * (ER1 + E1))
            sp.wait_ge(low_made, MIX_LOAD - 1)
            into_stage(1, mix_rows, D, MIX)
            for q in range(FOLDS):
                sp.wait_ge(low_made, PAIR_LOAD + q - 1)
                into_stage(q % 2, fold_tail[q], D)

            def load_tokens(t, par):
                sp.wait_ge(low_made, t + PAIR_LOAD + FOLDS - 1)
                into_stage(par, tokens[t], D)

            def store(t, j, odd):
                sp.wait_ge(read_out[TPAR[odd]], 3 * j + FOLD_PIECES[TPAR[odd]] + 3)
                sp.dma_start(out[bass.ds(t * P, P), :], rows[:, odd, :]).then_inc(rows_free[odd], 16)

            load_tokens(0, TPAR[0])
            load_tokens(1, TPAR[1])
            with sp.Fori(0, TILES // 2 - 1) as j:
                load_tokens(2 * j + 2, TPAR[0])
                store(2 * j, j, 0)
                load_tokens(2 * j + 3, TPAR[1])
                store(2 * j + 1, j, 1)
            store(TILES - 2, TILES // 2 - 1, 0)
            store(TILES - 1, TILES // 2 - 1, 1)
            sp.wait_ge(rows_free[0], 16 * (TILES // 2) + 1)
            sp.wait_ge(rows_free[1], 16 * (TILES // 2) + 1)

        @block.gpsimd
        def _(pool):
            nc.gpsimd.memset(ident[:, :], 0.0).then_inc(ident_zero, 1)
            pool.wait_ge(ident_zero, 1)
            nc.gpsimd.affine_select(out=ident[:, :], in_=ident[:, :], compare_op=ALU.not_equal, fill=1.0,
                                    base=0, pattern=[[-1, P]], channel_multiplier=1).then_inc(ident_made, 1)
            nc.gpsimd.iota(expert_no[:, :], pattern=[[1, E1]], base=0, channel_multiplier=0,
                           allow_small_or_imprecise_dtypes=True).then_inc(expert_made, 1)
            nc.gpsimd.memset(mix_is_low[:, :], 0.0).then_inc(mask_zero, 1)
            pool.wait_ge(mask_zero, 1)
            nc.gpsimd.memset(mix_is_low[ER2:2 * ER2, :], 1.0).then_inc(mask_zero, 1)
            pool.wait_ge(mask_zero, 2)
            nc.gpsimd.affine_select(out=mix_is_low[:, :], in_=mix_is_low[:, :], compare_op=ALU.not_equal, fill=1.0,
                                    base=-(MIX - 1), pattern=[[0, 1]], channel_multiplier=1).then_inc(mask_made, 1)
            pool.wait_ge(mask_made, 1)
            nc.gpsimd.tensor_scalar(mix_sign[:, :], mix_is_low[:, :], -2.0, 1.0, ALU.mult, ALU.add)\
                .then_inc(mask_sign, 1)

        @block.scalar
        def _(act):
            act.dma_start(lang_i[:, :], language).then_inc(lang_here, 16)

            def copy(out_, in_):
                return nc.scalar.activation(out_, in_, ACT.Copy)

            for k in range(KC):
                act.wait_ge(staged[k % HEAD_BUFS], 16 * (k // HEAD_BUFS + 1))
                copy(st_high[:, 0:HEAD_TILES, k, :],
                     stage[:, k % HEAD_BUFS, 0:HEAD_TILES * P].rearrange("p (s c) -> p s c", c=P))
                copy(m_high[:, k, :], stage[:, k % HEAD_BUFS, HEAD_TILES * P:HEAD_W]).then_inc(high_made, 1)
            act.wait_ge(staged[0], 16 * PAIR_STAGED)
            copy(c_high[:, 1:1 + KC, MCOLS:COLS],
                 stage[:, 0, 0:KC * (ER1 + E1)].rearrange("p (k c) -> p k c", k=KC)).then_inc(high_made, 1)
            act.wait_ge(staged[1], 16 * PAIR_STAGED)
            copy(mix[:, :], stage[0:MIX, 1, 0:D]).then_inc(high_made, 1)

            def round_tile(jq, par):
                act.wait_ge(staged[par], 16 * (PAIR_STAGED + 1) + 16 * jq)
                copy(st_high[:, SLOT[par], :, :].rearrange("p k c -> p (k c)"),
                     stage[:, par, 0:D]).then_inc(high_made, 1)

            def fold_out(s, par):
                act.wait_ge(contracted, s + 1)
                for p in ORDER:
                    a, b = FOLD_CUT[p], FOLD_CUT[p + 1]
                    copy(c_high[:, s, a:b], piece(par, p, 0, b - a)).then_inc(fold_high, 1)

            round_tile(0, 0)
            for s in range(HEAD_TILES):
                fold_out(s, s)
            with act.Fori(0, FOLDS // 2) as j:
                act.wait_ge(contracted, 2 * j + HEAD_TILES)
                round_tile(j, 1)
                fold_out(2 * j + HEAD_TILES, 0)
                round_tile(j + 1, 0)
                fold_out(2 * j + HEAD_TILES + 1, 1)
            act.wait_ge(contracted, HEAD_TILES + FOLDS - 1)
            round_tile(TPAIR[0], TPAR[0])
            fold_out(KC, 0)

            def round_next(t, j, odd):
                act.wait_ge(contracted, t + KC + 1)
                round_tile(j + 1 - (1 - odd) + TPAIR[1 - odd], TPAR[1 - odd])

            def token_tile(t, j, odd, with_next=True):
                par = TPAR[odd]
                if with_next:
                    round_next(t, j, odd)
                act.wait_ge(top_ready, t + 1)
                nc.scalar.activation(pair_exp[:, :], top[:, 0:1], ACT.Exp, bias=top[:, 1:2],
                                     scale=-1.0).then_inc(pair_exp_ready, 1)
                act.wait_ge(u_turned, t + 1)
                copy(ut_high[:, :], ut_psum).then_inc(ut_high_ready, 1)
                act.wait_ge(neg_max_ready, t + 1)
                nc.scalar.activation(y_exp[:, :], piece(par, 2, LOGIT2_AT, LOGIT2_AT + E2), ACT.Exp,
                                     bias=neg_max[:, 0:1], accum_out=y_sum[:, :]).then_inc(y_exp_ready, 1)
                act.wait_ge(v_turned, t + 1)
                copy(vt[:, :], vt_psum).then_inc(vt_ready, 1)
                act.wait_ge(rows_free[odd], 16 * j + 1)
                act.wait_ge(z_ready, 3 * t + 1)
                copy(rows[:, odd, 0:WIDE], piece(par, 0, 0, WIDE)).then_inc(read_out[par], 1)
                act.wait_ge(z_ready, 3 * t + 2)
                copy(rows[:, odd, 2 * WIDE:D], piece(par, 2, 0, Z_TAIL)).then_inc(read_out[par], 1)

            with act.Fori(0, TILES // 2 - 1) as j:
                token_tile(2 * j, j, 0)
                token_tile(2 * j + 1, j, 1)
            token_tile(TILES - 2, TILES // 2 - 1, 0)
            token_tile(TILES - 1, TILES // 2 - 1, 1, with_next=False)

        @block.vector
        def _(dve):
            dve.wait_ge(ident_made, 1)
            nc.vector.tensor_copy(ident_r[:, :], ident[:, :]).then_inc(ident_rounded, 1)
            for i in range(2):
                nc.vector.memset(v_rows[:, 3 * ER2 + i:3 * ER2 + i + 1], 1.0).then_inc(rows_free[i], 1)

            def low_part(dst, src, high):
                return nc.vector.tensor_tensor(dst, src, as_f32(high), ALU.subtract)

            for k in range(KC):
                buf = k % HEAD_BUFS
                dve.wait_ge(high_made, k + 1)
                low_part(st_low[:, 0:HEAD_TILES, k, :],
                         stage[:, buf, 0:HEAD_TILES * P].rearrange("p (s c) -> p s c", c=P),
                         st_high[:, 0:HEAD_TILES, k, :])
                low_part(m_low[:, k, :], stage[:, buf, HEAD_TILES * P:HEAD_W], m_high[:, k, :])\
                    .then_inc(low_made, 1)
            dve.wait_ge(high_made, GATE_LOAD + 1)
            low_part(c_low[:, 1:1 + KC, MCOLS:COLS],
                     stage[:, 0, 0:KC * (ER1 + E1)].rearrange("p (k c) -> p k c", k=KC),
                     c_high[:, 1:1 + KC, MCOLS:COLS]).then_inc(low_made, 1)
            dve.wait_ge(high_made, MIX_LOAD + 1)
            dve.wait_ge(mask_sign, 1)
            mix_staged = stage[0:MIX, 1, 0:D]
            nc.vector.tensor_scalar(mix_staged, mix_staged, mix_is_low[0:MIX, 0:1], None, ALU.mult)\
                .then_inc(mix_masked, 1)
            dve.wait_ge(mix_masked, 1)
            nc.vector.scalar_tensor_tensor(out=mix[:, :], in0=as_f32(mix[:, :]), scalar=mix_sign[0:MIX, 0:1],
                                           in1=mix_staged, op0=ALU.mult, op1=ALU.add).then_inc(low_made, 1)

            dve.wait_ge(lang_here, 16)
            dve.wait_ge(expert_made, 1)
            nc.vector.tensor_copy(lang_f[:, :], lang_i[:, :]).then_inc(vec, 1)
            dve.wait_ge(vec, 1)
            nc.vector.tensor_tensor(lang_bias[:, :, :], lang_f[:, :].unsqueeze(2).to_broadcast([P, TILES, E1]),
                                    expert_no[:, :].unsqueeze(1).to_broadcast([P, TILES, E1]),
                                    ALU.is_equal).then_inc(vec, 1)
            dve.wait_ge(vec, 2)
            nc.vector.tensor_scalar(lang_bias[:, :, :], lang_bias[:, :, :], LANG_BIAS, None, ALU.mult)\
                .then_inc(vec, 1)
            VEC_START = 3

            def low_tile(q, par):
                dve.wait_ge(high_made, q + PAIR_LOAD + 1)
                low_part(st_low[:, SLOT[par], :, :].rearrange("p k c -> p (k c)"), stage[:, par, 0:D],
                         st_high[:, SLOT[par], :, :].rearrange("p k c -> p (k c)")).then_inc(low_made, 1)

            def fold_out(s, par):
                for i, p in enumerate(ORDER):
                    a, b = FOLD_CUT[p], FOLD_CUT[p + 1]
                    dve.wait_ge(fold_high, 3 * s + i + 1)
                    low_part(c_low[:, s, a:b], piece(par, p, 0, b - a), c_high[:, s, a:b])\
                        .then_inc(read_out[par], 1)

            low_tile(0, 0)
            for s in range(HEAD_TILES):
                fold_out(s, s)
            with dve.Fori(0, FOLDS // 2) as j:
                low_tile(2 * j + 1, 1)
                fold_out(2 * j + HEAD_TILES, 0)
                low_tile(2 * j + 2, 0)
                fold_out(2 * j + HEAD_TILES + 1, 1)
            low_tile(FOLDS, TPAR[0])
            fold_out(KC, 0)

            STEPS = 11

            def token_tile(t, j, odd, with_next=True):
                par = TPAR[odd]
                base = STEPS * t + VEC_START
                step = [0]

                def link(ins):
                    step[0] += 1
                    ins.then_inc(vec, 1)
                    dve.wait_ge(vec, base + step[0])

                def narrow(a, b):
                    return piece(par, 2, a, b)

                dve.wait_ge(narrow_ready, t + 1)
                link(nc.vector.tensor_tensor(logits[:, :], narrow(LOGIT_AT, LOGIT_AT + E1),
                                             lang_bias[:, t, :], ALU.add))
                dve.sem_inc(carried, 1)
                link(nc.vector.max(top[:, :], logits[:, :]))
                dve.sem_inc(carried, 1)
                nc.vector.max_index(top_at[:, :], top[:, :], logits[:, :]).then_inc(top_ready, 1)
                dve.wait_ge(top_ready, t + 1)
                link(nc.vector.tensor_copy(top_at_f[:, :], top_at[:, 0:2]))
                dve.wait_ge(pair_exp_ready, t + 1)
                link(nc.vector.tensor_scalar(pair_half[:, :], pair_exp[:, :], 0.5, 0.5, ALU.mult, ALU.add))
                nc.vector.reciprocal(pair_scale[:, :], pair_half[:, :])
                link(nc.vector.tensor_scalar(gate_second[:, :], expert_no[:, :], top_at_f[:, 1:2], pair_exp[:, 0:1],
                                             ALU.is_equal, ALU.mult))
                link(nc.vector.scalar_tensor_tensor(out=gates[:, :], in0=expert_no[:, :], scalar=top_at_f[:, 0:1],
                                                    in1=gate_second[:, :], op0=ALU.is_equal, op1=ALU.add))
                nc.vector.scalar_tensor_tensor(
                    out=u[:, :].rearrange("p (e r) -> p e r", e=E1),
                    in0=narrow(PROJ_AT, PROJ_AT + ER1).rearrange("p (e r) -> p e r", e=E1),
                    scalar=pair_scale[:, 0:1], in1=gates[:, :].unsqueeze(2).to_broadcast([P, E1, R1]),
                    op0=ALU.mult, op1=ALU.mult).then_inc(u_ready, 1)
                dve.wait_ge(ut_high_ready, t + 1)
                low_part(ut_low[:, :], ut_psum, ut_high[:, :]).then_inc(ut_low_ready, 1)
                dve.wait_ge(y_small_ready, t + 1)
                nc.vector.tensor_reduce(neg_max[:, :], narrow(LOGIT2_AT, LOGIT2_AT + E2), AX.X, ALU.max,
                                        negate=True).then_inc(neg_max_ready, 1)
                dve.wait_ge(y_exp_ready, t + 1)
                link(nc.vector.tensor_scalar(y_half[:, :], y_sum[:, :], 0.5, None, ALU.mult))
                link(nc.vector.reciprocal(y_scale[:, :], y_half[:, :]))
                link(nc.vector.scalar_tensor_tensor(
                    out=v[:, :].rearrange("p (e r) -> p e r", e=E2),
                    in0=narrow(PROJ2_AT, PROJ2_AT + ER2).rearrange("p (e r) -> p e r", e=E2),
                    scalar=y_scale[:, 0:1], in1=y_exp[:, :].unsqueeze(2).to_broadcast([P, E2, R2]),
                    op0=ALU.mult, op1=ALU.mult))
                link(nc.vector.tensor_copy(
                    v_rows[:, 0:2 * ER2].bitcast(F32R).rearrange("p (a c) -> p a c", a=2),
                    v[:, :].unsqueeze(1).to_broadcast([P, 2, ER2])))
                link(nc.vector.tensor_tensor(v_rows[:, 2 * ER2:3 * ER2], v[:, :], v_rows[:, 0:ER2], ALU.subtract))
                assert step[0] == STEPS, step
                dve.sem_inc(v_ready, 1)
                if with_next:
                    low_tile(t + FOLDS + 1, TPAR[1 - odd])
                dve.wait_ge(rows_free[odd], 16 * j + 1)
                dve.wait_ge(z_ready, 3 * t + 3)
                nc.vector.tensor_copy(rows[:, odd, WIDE:2 * WIDE], piece(par, 1, 0, WIDE))\
                    .then_inc(read_out[par], 1)

            with dve.Fori(0, TILES // 2 - 1) as j:
                token_tile(2 * j, j, 0)
                token_tile(2 * j + 1, j, 1)
            token_tile(TILES - 2, TILES // 2 - 1, 0)
            token_tile(TILES - 1, TILES // 2 - 1, 1, with_next=False)

        @block.tensor
        def _(pe):
            def mm(out_, lhs, rhs, start=False, stop=False):
                return nc.tensor.matmul(out_, lhs, rhs, start=start, stop=stop, skip_group_check=True)

            HH, HL, LH = range(3)

            def product(kind, slot, k, par, p, cut, high, low):
                lhs = (st_high, st_high, st_low)[kind]
                rhs = (high, low, high)[kind]
                return mm(piece(par, p, 0, cut[p + 1] - cut[p]), lhs[:, slot, k, :], rhs[:, cut[p]:cut[p + 1]],
                          start=k == 0 and kind == HH, stop=k == KC - 1 and kind == LH)

            pe.wait_ge(ident_rounded, 1)
            for k in range(KC):
                for kind in (HH, HL, LH):
                    if kind == HH:
                        pe.wait_ge(high_made, k + 1)
                    if kind == HL:
                        pe.wait_ge(low_made, k + 1)
                    for s in range(HEAD_TILES):
                        if kind != LH or k < KC - 1:
                            for p in ORDER:
                                product(kind, s, k, s, p, FOLD_CUT, m_high[:, k, :], m_low[:, k, :])
            for s in range(HEAD_TILES):
                for p in ORDER:
                    last = product(LH, s, KC - 1, s, p, FOLD_CUT, m_high[:, KC - 1, :], m_low[:, KC - 1, :])
                if s > 0:
                    last = mm(piece(s, (s - 1) // 3, (s - 1) % 3 * P, ((s - 1) % 3 + 1) * P),
                              ident_r[:, :], ident_r[:, :])
                last.then_inc(contracted, 1)

            def fold_tile(s, jq, par, ready=3):
                pe.wait_ge(low_made, s - HEAD_TILES + PAIR_LOAD + 1)
                for k in range(KC):
                    for kind in (HH, HL, LH):
                        for i, p in enumerate(ORDER):
                            if k == 0 and kind == HH:
                                pe.wait_ge(read_out[par], 3 * jq + i + 1)
                            product(kind, SLOT[par], k, par, p, FOLD_CUT, m_high[:, k, :], m_low[:, k, :])
                d = s - 1
                mm(sums[:, 3 * par + d // 3, bass.ds(d % 3 * P, P)], ident_r[:, :], ident_r[:, :])\
                    .then_inc(contracted, 1)

            with pe.Fori(0, FOLDS // 2) as j:
                fold_tile(2 * j + HEAD_TILES, j, 0)
                fold_tile(2 * j + HEAD_TILES + 1, j, 1)
            fold_tile(KC, FOLDS // 2, 0)

            def token_tile(t, j, odd):
                par = TPAR[odd]
                slot = SLOT[par]

                def chunk(k, pieces):
                    for kind in (HH, HL, LH):
                        for p in pieces:
                            last = product(kind, slot, k, par, p, TOKEN_CUT, c_high[:, 1 + k, :], c_low[:, 1 + k, :])
                    return last

                pe.wait_ge(low_made, t + PAIR_LOAD + FOLDS + 1)
                pe.wait_ge(read_out[par], 3 * j + FOLD_PIECES[par])
                for k in range(KC):
                    if k == KC - 1:
                        pe.wait_ge(read_out[0], FOLD_PIECES[0] - 2)
                    last = chunk(k, (2,))
                last.then_inc(narrow_ready, 1)
                for k in range(3):
                    chunk(k, (0, 1))
                pe.wait_ge(u_ready, t + 1)
                nc.tensor.transpose(ut_psum, u[:, :], ident[:, :]).then_inc(u_turned, 1)
                for k in range(3, 5):
                    chunk(k, (0, 1))
                pe.wait_ge(ut_low_ready, t + 1)
                parts = ((ut_high, c_high), (ut_high, c_low), (ut_low, c_high))
                for lhs, rhs in parts:
                    last = mm(piece(par, 2, 0, MCOLS - 2 * WIDE), lhs[:, :], rhs[:, 0, 2 * WIDE:MCOLS])
                last.then_inc(y_small_ready, 1)
                for k in range(5, KC):
                    if k == KC - 1:
                        pe.wait_ge(read_out[0], FOLD_PIECES[0])
                    last = chunk(k, (0, 1))
                last.then_inc(contracted, 1)
                pe.wait_ge(v_ready, t + 1)
                nc.tensor.transpose(vt_psum, v_rows[:, :], ident[:, :]).then_inc(v_turned, 1)
                for lhs, rhs in parts:
                    for p in (0, 1):
                        mm(piece(par, p, 0, WIDE), lhs[:, :], rhs[:, 0, p * WIDE:(p + 1) * WIDE])
                pe.wait_ge(vt_ready, t + 1)
                for p, a, b in ((0, 0, WIDE), (2, 2 * WIDE, D), (1, WIDE, 2 * WIDE)):
                    mm(piece(par, p, 0, b - a), vt[:, :], mix[:, a:b]).then_inc(z_ready, 1)

            with pe.Fori(0, TILES // 2) as j:
                token_tile(2 * j, j, 0)
                token_tile(2 * j + 1, j, 1)


def kernel(**inputs):
    import numpy as np
    import concourse.bacc as bacc
    from concourse.bass_utils import run_bass_kernel_spmd

    P = 128
    x = np.asarray(inputs["x"])
    batch, seq, D = x.shape
    KC = D // P
    tokens = batch * seq
    tiles = tokens // P
    W, Wr, A, B = (np.asarray(inputs["L0_cond_" + n]) for n in ("W", "Wr", "A", "B"))
    Wf, bf, Af, Bm, Wrf = (np.asarray(inputs["L0_ffn_" + n]) for n in ("W", "b", "A", "Bm", "Wr"))

    m_t = np.concatenate([Wf, Wrf, Af.reshape(-1, D)], axis=0).T
    b_t = B.transpose(1, 0, 2).reshape(D, -1)
    head = np.concatenate([b_t, W[:, :P], m_t], axis=1).reshape(KC, P, -1)
    fold_tail = W[:, P:].reshape(KC, P, KC - 1, P).transpose(2, 1, 0, 3).reshape(KC - 1, P, D)
    x_t = x.reshape(tiles, P, KC, P).transpose(0, 3, 2, 1).reshape(tiles, P, D)
    gate_proj = np.concatenate([A.reshape(-1, D), Wr], axis=0).T.reshape(KC, P, -1).transpose(1, 0, 2)
    bm_t = Bm.transpose(0, 2, 1).reshape(-1, D)
    mix_rows = np.concatenate([bm_t, bm_t, bm_t, bf[None], bf[None]], axis=0)
    language = np.repeat(np.asarray(inputs["itok_B_0_7"]), seq).reshape(tiles, P).T

    arrays = dict(head=head, fold_tail=fold_tail, tokens=x_t, gate_proj=gate_proj, mix_rows=mix_rows,
                  language=language)
    arrays = {n: np.ascontiguousarray(a) for n, a in arrays.items()}
    nc = bacc.Bacc("TRN2", target_bir_lowering=False, num_devices=1)
    args = [nc.dram_tensor(n, a.shape, mybir.dt.from_np(a.dtype), kind="ExternalInput").ap()
            for n, a in arrays.items()]
    out = nc.dram_tensor("out", (tokens, D), mybir.dt.float32, kind="ExternalOutput").ap()
    adaln_ffn_kernel(nc, *args, out)
    r = run_bass_kernel_spmd(nc, [arrays], core_ids=[0])
    return r.results[0]["out"].reshape(batch, seq, D)
```

```python
import concourse.bass as bass
from concourse import mybir
from contextlib import ExitStack



def adaln_ffn_kernel(nc, head, fold_tail, tokens, gate_proj, mix_rows, language, out):
    F32 = mybir.dt.float32
    F32R = mybir.dt.float32r
    I32 = mybir.dt.int32
    U32 = mybir.dt.uint32
    ALU = mybir.AluOpType
    ACT = mybir.ActivationFunctionType
    AX = mybir.AxisListType

    P = 128
    BANK = 512
    D = out.shape[1]
    KC = D // P
    TILES = out.shape[0] // P
    HEAD_TILES = 2
    HEAD_W = head.shape[2]
    MCOLS = HEAD_W - HEAD_TILES * P
    E1 = 8
    ER1 = gate_proj.shape[2] - E1
    R1 = ER1 // E1
    E2 = 4
    SMALL2 = MCOLS - D
    ER2 = SMALL2 - E2
    R2 = ER2 // E2
    COLS = MCOLS + ER1 + E1
    MIX = mix_rows.shape[0]
    LANG_BIAS = 5.0

    WIDE = 3 * P
    FOLD_CUT = (0, WIDE, 2 * WIDE, MCOLS)
    TOKEN_CUT = (0, WIDE, 2 * WIDE, COLS)
    Z_TAIL = D - 2 * WIDE
    LOGIT2_AT = Z_TAIL
    PROJ2_AT = LOGIT2_AT + E2
    PROJ_AT = Z_TAIL + SMALL2
    LOGIT_AT = PROJ_AT + ER1
    TURN_AT, LORA_AT = 10, 16
    WARM_UP = 6
    ORDER = (2, 0, 1)

    HEAD_BUFS = 3
    FIRST_PART = FOLD_CUT[2]
    HEAD_LOADS = KC + 1
    PAIR_STAGED = (KC + 2) // 3
    FOLDS = KC + 1 - HEAD_TILES
    SLOT = (2, 0)
    FOLD_PIECES = (3 * (1 + (FOLDS + 1) // 2), 3 * (1 + FOLDS // 2))

    ctx = ExitStack()
    with ctx:
        def sb(name, shape, dt=F32):
            return ctx.enter_context(nc.sbuf_tensor(name, shape, dt))

        def sem(name):
            return ctx.enter_context(nc.semaphore(name))

        c_high = sb("c_high", [P, 1 + KC, COLS], F32R)
        c_low = sb("c_low", [P, 1 + KC, COLS], F32R)
        st_high = sb("st_high", [P, 3, KC, P], F32R)
        st_low = sb("st_low", [P, 3, KC, P], F32R)
        stage = sb("stage", [P, HEAD_BUFS, HEAD_W])
        mix = sb("mix", [MIX, D], F32R)
        mix_is_low = sb("mix_is_low", [P, 1])
        mix_sign = sb("mix_sign", [P, 1])
        ident = sb("ident", [P, P])
        ident_r = sb("ident_r", [P, P], F32R)
        lang_i = sb("lang_i", [P, TILES], I32)
        lang_f = sb("lang_f", [P, TILES])
        expert_no = sb("expert_no", [P, E1])
        lang_bias = sb("lang_bias", [P, TILES, E1])
        logits = sb("logits", [P, E1])
        top = sb("top", [P, E1])
        top_at = sb("top_at", [P, E1], U32)
        top_at_f = sb("top_at_f", [P, 2])
        pair_exp = sb("pair_exp", [P, 1])
        pair_half = sb("pair_half", [P, 1])
        pair_scale = sb("pair_scale", [P, 1])
        gate_second = sb("gate_second", [P, E1])
        gates = sb("gates", [P, E1])
        u = sb("u", [P, ER1])
        ut_high = sb("ut_high", [P, P], F32R)
        ut_low = sb("ut_low", [P, P], F32R)
        neg_max = sb("neg_max", [P, 1])
        y_exp = sb("y_exp", [P, E2])
        y_sum = sb("y_sum", [P, 1])
        y_scale = sb("y_scale", [P, 1])
        v = sb("v", [P, ER2])
        v_rows = sb("v_rows", [P, MIX])
        vt = sb("vt", [MIX, P], F32R)
        with nc.sbuf_tensor("m_high", [P, KC, MCOLS], F32R) as m_high, \
                nc.sbuf_tensor("m_low", [P, KC, MCOLS], F32R) as m_low:
            pass
        rows = sb("rows", [P, 2, D])

        sums = ctx.enter_context(nc.psum_tensor("sums", [P, 6, BANK], F32))
        turned = ctx.enter_context(nc.psum_tensor("turned", [P, 2, BANK], F32))
        ut_psum = turned[:, 0, 0:P]
        vt_psum = turned[0:MIX, 1, 0:P]

        staged = [sem(f"staged_{i}") for i in range(HEAD_BUFS)]
        first_staged = sem("first_staged")
        lang_here = sem("lang_here")
        ident_zero = sem("ident_zero")
        ident_made = sem("ident_made")
        ident_rounded = sem("ident_rounded")
        mask_zero = sem("mask_zero")
        mask_made = sem("mask_made")
        mask_sign = sem("mask_sign")
        expert_made = sem("expert_made")
        high_made = sem("high_made")
        low_made = sem("low_made")
        gate_high = sem("gate_high")
        gate_split = sem("gate_split")
        mix_high = sem("mix_high")
        mix_masked = sem("mix_masked")
        mix_split = sem("mix_split")
        warm = sem("warm")
        contracted = sem("contracted")
        fold_high = sem("fold_high")
        read_out = [sem("read_out_0"), sem("read_out_1")]
        vec = sem("vec")
        carried = sem("carried")
        narrow_ready = sem("narrow_ready")
        top_ready = sem("top_ready")
        pair_exp_ready = sem("pair_exp_ready")
        u_ready = sem("u_ready")
        u_turned = sem("u_turned")
        ut_high_ready = sem("ut_high_ready")
        ut_low_ready = sem("ut_low_ready")
        y_small_ready = sem("y_small_ready")
        neg_max_ready = sem("neg_max_ready")
        y_exp_ready = sem("y_exp_ready")
        v_ready = sem("v_ready")
        v_turned = sem("v_turned")
        vt_ready = sem("vt_ready")
        z_ready = sem("z_ready")
        rows_free = [sem("rows_free_0"), sem("rows_free_1")]

        def as_f32(t):
            return t.bitcast(F32)

        def piece(par, p, a=0, b=BANK):
            return sums[:, 3 * par + p, a:b]

        TPAR = (1, 0)
        TPAIR = (FOLDS // 2, (FOLDS + 1) // 2)

        block = ctx.enter_context(nc.Block())

        @block.sync
        def _(sp):
            def into_stage(buf, src, width, part=P):
                sp.dma_start(stage[0:part, buf, 0:width], src).then_inc(staged[buf], 16)

            sp.dma_start(stage[:, 0, FIRST_PART:HEAD_W], head[0, :, FIRST_PART:HEAD_W]).then_inc(first_staged, 16)
            into_stage(0, head[0, :, 0:FIRST_PART], FIRST_PART)
            for k in range(1, KC):
                if k >= HEAD_BUFS:
                    sp.wait_ge(low_made, k - HEAD_BUFS + 2)
                into_stage(k % HEAD_BUFS, head[k], HEAD_W)
            sp.wait_ge(low_made, HEAD_LOADS - 2)
            into_stage(2, gate_proj.rearrange("p k c -> p (k c)"), KC * (ER1 + E1))
            for q in range(2):
                sp.wait_ge(low_made, HEAD_LOADS + q - 1)
                into_stage(q, fold_tail[q], D)
            sp.wait_ge(gate_split, 1)
            into_stage(2, mix_rows, D, MIX)
            for q in range(2, FOLDS):
                sp.wait_ge(low_made, HEAD_LOADS + q - 1)
                into_stage(q % 2, fold_tail[q], D)

            def load_tokens(t, par):
                sp.wait_ge(low_made, t + HEAD_LOADS + FOLDS - 1)
                into_stage(par, tokens[t], D)

            def store(t, j, odd):
                sp.wait_ge(read_out[TPAR[odd]], 3 * j + FOLD_PIECES[TPAR[odd]] + 3)
                sp.dma_start(out[bass.ds(t * P, P), :], rows[:, odd, :]).then_inc(rows_free[odd], 16)

            load_tokens(0, TPAR[0])
            load_tokens(1, TPAR[1])
            with sp.Fori(0, TILES // 2 - 1) as j:
                load_tokens(2 * j + 2, TPAR[0])
                store(2 * j, j, 0)
                load_tokens(2 * j + 3, TPAR[1])
                store(2 * j + 1, j, 1)
            store(TILES - 2, TILES // 2 - 1, 0)
            store(TILES - 1, TILES // 2 - 1, 1)
            sp.wait_ge(rows_free[0], 16 * (TILES // 2) + 1)
            sp.wait_ge(rows_free[1], 16 * (TILES // 2) + 1)

        @block.gpsimd
        def _(pool):
            nc.gpsimd.memset(ident[:, :], 0.0).then_inc(ident_zero, 1)
            pool.wait_ge(ident_zero, 1)
            nc.gpsimd.affine_select(out=ident[:, :], in_=ident[:, :], compare_op=ALU.not_equal, fill=1.0,
                                    base=0, pattern=[[-1, P]], channel_multiplier=1).then_inc(ident_made, 1)
            nc.gpsimd.iota(expert_no[:, :], pattern=[[1, E1]], base=0, channel_multiplier=0,
                           allow_small_or_imprecise_dtypes=True).then_inc(expert_made, 1)
            nc.gpsimd.memset(mix_is_low[:, :], 0.0).then_inc(mask_zero, 1)
            pool.wait_ge(mask_zero, 1)
            nc.gpsimd.memset(mix_is_low[ER2:2 * ER2, :], 1.0).then_inc(mask_zero, 1)
            pool.wait_ge(mask_zero, 2)
            nc.gpsimd.affine_select(out=mix_is_low[:, :], in_=mix_is_low[:, :], compare_op=ALU.not_equal, fill=1.0,
                                    base=-(MIX - 1), pattern=[[0, 1]], channel_multiplier=1).then_inc(mask_made, 1)
            pool.wait_ge(mask_made, 1)
            nc.gpsimd.tensor_scalar(mix_sign[:, :], mix_is_low[:, :], -2.0, 1.0, ALU.mult, ALU.add)\
                .then_inc(mask_sign, 1)

        @block.scalar
        def _(act):
            act.dma_start(lang_i[:, :], language).then_inc(lang_here, 16)

            def copy(out_, in_):
                return nc.scalar.activation(out_, in_, ACT.Copy)

            for k in range(KC):
                act.wait_ge(*((first_staged, 16) if k == 0 else (staged[k % HEAD_BUFS], 16 * (k // HEAD_BUFS + 1))))
                copy(st_high[:, 0:HEAD_TILES, k, :],
                     stage[:, k % HEAD_BUFS, MCOLS:HEAD_W].rearrange("p (s c) -> p s c", c=P))
                if k == 0:
                    copy(m_high[:, 0, FIRST_PART:MCOLS], stage[:, 0, FIRST_PART:MCOLS]).then_inc(high_made, 1)
                    act.wait_ge(staged[0], 16)
                    copy(m_high[:, 0, 0:FIRST_PART], stage[:, 0, 0:FIRST_PART]).then_inc(high_made, 1)
                else:
                    copy(m_high[:, k, :], stage[:, k % HEAD_BUFS, 0:MCOLS]).then_inc(high_made, 1)

            def round_tile(jq, par):
                act.wait_ge(staged[par], 16 * (PAIR_STAGED + 1) + 16 * jq)
                copy(st_high[:, SLOT[par], :, :].rearrange("p k c -> p (k c)"),
                     stage[:, par, 0:D]).then_inc(high_made, 1)

            def fold_out(s, par):
                act.wait_ge(contracted, s + 1)
                for p in ORDER:
                    a, b = FOLD_CUT[p], FOLD_CUT[p + 1]
                    copy(c_high[:, s, a:b], piece(par, p, 0, b - a)).then_inc(fold_high, 1)

            round_tile(0, 0)
            act.wait_ge(staged[2], 16 * (KC // HEAD_BUFS + 1))
            copy(c_high[:, 1:1 + KC, MCOLS:COLS],
                 stage[:, 2, 0:KC * (ER1 + E1)].rearrange("p (k c) -> p k c", k=KC)).then_inc(gate_high, 1)
            for s in range(HEAD_TILES):
                fold_out(s, s)
            act.wait_ge(staged[2], 16 * (KC // HEAD_BUFS + 2))
            copy(mix[:, :], stage[0:MIX, 2, 0:D]).then_inc(mix_high, 1)
            with act.Fori(0, FOLDS // 2) as j:
                act.wait_ge(contracted, 2 * j + HEAD_TILES)
                round_tile(j, 1)
                fold_out(2 * j + HEAD_TILES, 0)
                round_tile(j + 1, 0)
                fold_out(2 * j + HEAD_TILES + 1, 1)
            act.wait_ge(contracted, HEAD_TILES + FOLDS - 1)
            round_tile(TPAIR[0], TPAR[0])
            fold_out(KC, 0)

            def round_next(t, j, odd):
                act.wait_ge(contracted, t + KC + 1)
                round_tile(j + odd + TPAIR[1 - odd], TPAR[1 - odd])

            def token_tile(t, j, odd, with_next=True):
                par = TPAR[odd]
                if with_next:
                    round_next(t, j, odd)
                act.wait_ge(top_ready, t + 1)
                nc.scalar.activation(pair_exp[:, :], top[:, 0:1], ACT.Exp, bias=top[:, 1:2],
                                     scale=-1.0).then_inc(pair_exp_ready, 1)
                act.wait_ge(u_turned, t + 1)
                copy(ut_high[:, :], ut_psum).then_inc(ut_high_ready, 1)
                act.wait_ge(neg_max_ready, t + 1)
                nc.scalar.activation(y_exp[:, :], piece(par, 2, LOGIT2_AT, LOGIT2_AT + E2), ACT.Exp,
                                     bias=neg_max[:, 0:1], accum_out=y_sum[:, :]).then_inc(y_exp_ready, 1)
                act.wait_ge(v_turned, t + 1)
                copy(vt[:, :], vt_psum).then_inc(vt_ready, 1)
                act.wait_ge(rows_free[odd], 16 * j + 1)
                act.wait_ge(z_ready, 3 * t + 1)
                copy(rows[:, odd, 0:WIDE], piece(par, 0, 0, WIDE)).then_inc(read_out[par], 1)
                act.wait_ge(z_ready, 3 * t + 2)
                copy(rows[:, odd, 2 * WIDE:D], piece(par, 2, 0, Z_TAIL)).then_inc(read_out[par], 1)

            with act.Fori(0, TILES // 2 - 1) as j:
                token_tile(2 * j, j, 0)
                token_tile(2 * j + 1, j, 1)
            token_tile(TILES - 2, TILES // 2 - 1, 0)
            token_tile(TILES - 1, TILES // 2 - 1, 1, with_next=False)

        @block.vector
        def _(dve):
            dve.wait_ge(ident_made, 1)
            nc.vector.tensor_copy(ident_r[:, :], ident[:, :]).then_inc(ident_rounded, 1)
            for i in range(2):
                nc.vector.memset(v_rows[:, 3 * ER2 + i:3 * ER2 + i + 1], 1.0).then_inc(rows_free[i], 1)

            def low_part(dst, src, high):
                return nc.vector.tensor_tensor(dst, src, as_f32(high), ALU.subtract)

            for k in range(KC):
                buf = k % HEAD_BUFS
                dve.wait_ge(high_made, 1 if k == 0 else k + 2)
                low_part(st_low[:, 0:HEAD_TILES, k, :],
                         stage[:, buf, MCOLS:HEAD_W].rearrange("p (s c) -> p s c", c=P),
                         st_high[:, 0:HEAD_TILES, k, :])
                if k == 0:
                    low_part(m_low[:, 0, FIRST_PART:MCOLS], stage[:, 0, FIRST_PART:MCOLS],
                             m_high[:, 0, FIRST_PART:MCOLS]).then_inc(low_made, 1)
                    dve.wait_ge(high_made, 2)
                    low_part(m_low[:, 0, 0:FIRST_PART], stage[:, 0, 0:FIRST_PART], m_high[:, 0, 0:FIRST_PART])\
                        .then_inc(low_made, 1)
                else:
                    low_part(m_low[:, k, :], stage[:, buf, 0:MCOLS], m_high[:, k, :]).then_inc(low_made, 1)

            def low_tile(q, par):
                dve.wait_ge(high_made, q + HEAD_LOADS + 1)
                low_part(st_low[:, SLOT[par], :, :].rearrange("p k c -> p (k c)"), stage[:, par, 0:D],
                         st_high[:, SLOT[par], :, :].rearrange("p k c -> p (k c)")).then_inc(low_made, 1)

            low_tile(0, 0)
            dve.wait_ge(gate_high, 1)
            low_part(c_low[:, 1:1 + KC, MCOLS:COLS],
                     stage[:, 2, 0:KC * (ER1 + E1)].rearrange("p (k c) -> p k c", k=KC),
                     c_high[:, 1:1 + KC, MCOLS:COLS]).then_inc(gate_split, 1)

            def fold_out(s, par):
                for i, p in enumerate(ORDER):
                    a, b = FOLD_CUT[p], FOLD_CUT[p + 1]
                    dve.wait_ge(fold_high, 3 * s + i + 1)
                    low_part(c_low[:, s, a:b], piece(par, p, 0, b - a), c_high[:, s, a:b])\
                        .then_inc(read_out[par], 1)

            for s in range(HEAD_TILES):
                fold_out(s, s)
            dve.wait_ge(mix_high, 1)
            dve.wait_ge(mask_sign, 1)
            mix_staged = stage[0:MIX, 2, 0:D]
            nc.vector.tensor_scalar(mix_staged, mix_staged, mix_is_low[0:MIX, 0:1], None, ALU.mult)\
                .then_inc(mix_masked, 1)
            dve.wait_ge(mix_masked, 1)
            nc.vector.scalar_tensor_tensor(out=mix[:, :], in0=as_f32(mix[:, :]), scalar=mix_sign[0:MIX, 0:1],
                                           in1=mix_staged, op0=ALU.mult, op1=ALU.add).then_inc(mix_split, 1)
            dve.wait_ge(lang_here, 16)
            dve.wait_ge(expert_made, 1)
            nc.vector.tensor_copy(lang_f[:, :], lang_i[:, :]).then_inc(vec, 1)
            dve.wait_ge(vec, 1)
            nc.vector.tensor_tensor(lang_bias[:, :, :], lang_f[:, :].unsqueeze(2).to_broadcast([P, TILES, E1]),
                                    expert_no[:, :].unsqueeze(1).to_broadcast([P, TILES, E1]),
                                    ALU.is_equal).then_inc(vec, 1)
            dve.wait_ge(vec, 2)
            nc.vector.tensor_scalar(lang_bias[:, :, :], lang_bias[:, :, :], LANG_BIAS, None, ALU.mult)\
                .then_inc(vec, 1)
            VEC_START = 3

            with dve.Fori(0, FOLDS // 2) as j:
                low_tile(2 * j + 1, 1)
                fold_out(2 * j + HEAD_TILES, 0)
                low_tile(2 * j + 2, 0)
                fold_out(2 * j + HEAD_TILES + 1, 1)
            low_tile(FOLDS, TPAR[0])
            fold_out(KC, 0)

            STEPS = 11

            def token_tile(t, j, odd, with_next=True):
                par = TPAR[odd]
                base = STEPS * t + VEC_START
                step = [0]

                def put(ins):
                    step[0] += 1
                    ins.then_inc(vec, 1)

                def link(ins):
                    put(ins)
                    dve.wait_ge(vec, base + step[0])

                def narrow(a, b):
                    return piece(par, 2, a, b)

                dve.wait_ge(narrow_ready, t + 1)
                link(nc.vector.tensor_tensor(logits[:, :], narrow(LOGIT_AT, LOGIT_AT + E1),
                                             lang_bias[:, t, :], ALU.add))
                dve.sem_inc(carried, 1)
                link(nc.vector.max(top[:, :], logits[:, :]))
                dve.sem_inc(carried, 1)
                nc.vector.max_index(top_at[:, :], top[:, :], logits[:, :]).then_inc(top_ready, 1)
                dve.wait_ge(top_ready, t + 1)
                link(nc.vector.tensor_copy(top_at_f[:, :], top_at[:, 0:2]))
                dve.wait_ge(pair_exp_ready, t + 1)
                put(nc.vector.tensor_scalar(pair_half[:, :], pair_exp[:, :], 0.5, 0.5, ALU.mult, ALU.add))
                link(nc.vector.tensor_scalar(gate_second[:, :], expert_no[:, :], top_at_f[:, 1:2], pair_exp[:, 0:1],
                                             ALU.is_equal, ALU.mult))
                put(nc.vector.reciprocal(pair_scale[:, :], pair_half[:, :]))
                link(nc.vector.scalar_tensor_tensor(out=gates[:, :], in0=expert_no[:, :], scalar=top_at_f[:, 0:1],
                                                    in1=gate_second[:, :], op0=ALU.is_equal, op1=ALU.add))
                nc.vector.scalar_tensor_tensor(
                    out=u[:, :].rearrange("p (e r) -> p e r", e=E1),
                    in0=narrow(PROJ_AT, PROJ_AT + ER1).rearrange("p (e r) -> p e r", e=E1),
                    scalar=pair_scale[:, 0:1], in1=gates[:, :].unsqueeze(2).to_broadcast([P, E1, R1]),
                    op0=ALU.mult, op1=ALU.mult).then_inc(u_ready, 1)
                dve.wait_ge(ut_high_ready, t + 1)
                low_part(ut_low[:, :], ut_psum, ut_high[:, :]).then_inc(ut_low_ready, 1)
                dve.wait_ge(y_small_ready, t + 1)
                nc.vector.tensor_reduce(neg_max[:, :], narrow(LOGIT2_AT, LOGIT2_AT + E2), AX.X, ALU.max,
                                        negate=True).then_inc(neg_max_ready, 1)
                dve.wait_ge(y_exp_ready, t + 1)
                link(nc.vector.reciprocal(y_scale[:, :], y_sum[:, :]))
                link(nc.vector.scalar_tensor_tensor(
                    out=v[:, :].rearrange("p (e r) -> p e r", e=E2),
                    in0=narrow(PROJ2_AT, PROJ2_AT + ER2).rearrange("p (e r) -> p e r", e=E2),
                    scalar=y_scale[:, 0:1], in1=y_exp[:, :].unsqueeze(2).to_broadcast([P, E2, R2]),
                    op0=ALU.mult, op1=ALU.mult))
                link(nc.vector.tensor_scalar(
                    v_rows[:, 0:2 * ER2].bitcast(F32R).rearrange("p (a c) -> p a c", a=2),
                    v[:, :].unsqueeze(1).to_broadcast([P, 2, ER2]), 2.0, None, ALU.mult))
                link(nc.vector.scalar_tensor_tensor(out=v_rows[:, 2 * ER2:3 * ER2], in0=v[:, :], scalar=2.0,
                                                    in1=v_rows[:, 0:ER2], op0=ALU.mult, op1=ALU.subtract))
                assert step[0] == STEPS, step
                dve.sem_inc(v_ready, 1)
                if with_next:
                    low_tile(t + FOLDS + 1, TPAR[1 - odd])
                dve.wait_ge(rows_free[odd], 16 * j + 1)
                dve.wait_ge(z_ready, 3 * t + 3)
                nc.vector.tensor_copy(rows[:, odd, WIDE:2 * WIDE], piece(par, 1, 0, WIDE))\
                    .then_inc(read_out[par], 1)

            with dve.Fori(0, TILES // 2 - 1) as j:
                token_tile(2 * j, j, 0)
                token_tile(2 * j + 1, j, 1)
            token_tile(TILES - 2, TILES // 2 - 1, 0)
            token_tile(TILES - 1, TILES // 2 - 1, 1, with_next=False)

        @block.tensor
        def _(pe):
            def mm(out_, lhs, rhs, start=False, stop=False):
                return nc.tensor.matmul(out_, lhs, rhs, start=start, stop=stop, skip_group_check=True)

            def pe_loop(count):
                return nc.Fori(0, count, engines=(mybir.EngineType.PE,), hint_back_edge=True)

            HH, HL, LH = range(3)

            def product(kind, slot, k, par, p, cut, high, low):
                lhs = (st_high, st_high, st_low)[kind]
                rhs = (high, low, high)[kind]
                return mm(piece(par, p, 0, cut[p + 1] - cut[p]), lhs[:, slot, k, :], rhs[:, cut[p]:cut[p + 1]],
                          start=k == 0 and kind == HH, stop=k == KC - 1 and kind == LH)

            pe.wait_ge(ident_rounded, 1)
            for _ in range(WARM_UP):
                last = mm(turned[:, 1, :].rearrange("p (a c) -> p a c", a=4), ident_r[:, :],
                          ident_r[:, :].unsqueeze(1).to_broadcast([P, 4, P]), start=True, stop=True)
            last.then_inc(warm, 1)

            def head_products(kind, s, k, pieces):
                for p in pieces:
                    last = product(kind, s, k, s, p, FOLD_CUT, m_high[:, k, :], m_low[:, k, :])
                return last

            for part, pieces in enumerate(((2,), (0, 1))):
                for kind in (HH, HL, LH):
                    if kind != LH:
                        pe.wait_ge(high_made if kind == HH else low_made, part + 1)
                    for s in range(HEAD_TILES):
                        head_products(kind, s, 0, pieces)
            for k in range(1, KC - 1):
                for kind in (HH, HL, LH):
                    if kind != LH:
                        pe.wait_ge(high_made if kind == HH else low_made, k + 2)
                    for s in range(HEAD_TILES):
                        head_products(kind, s, k, ORDER)
            pe.wait_ge(low_made, KC + 1)
            for s in range(HEAD_TILES):
                for kind in (HH, HL, LH):
                    last = head_products(kind, s, KC - 1, ORDER)
                if s > 0:
                    last = mm(piece(s, (s - 1) // 3, (s - 1) % 3 * P, ((s - 1) % 3 + 1) * P),
                              ident_r[:, :], ident_r[:, :])
                last.then_inc(contracted, 1)

            def fold_tile(s, jq, par):
                pe.wait_ge(low_made, s - HEAD_TILES + HEAD_LOADS + 1)
                for k in range(KC):
                    for kind in (HH, HL, LH):
                        for i, p in enumerate(ORDER):
                            if k == 0 and kind == HH:
                                pe.wait_ge(read_out[par], 3 * jq + i + 1)
                            product(kind, SLOT[par], k, par, p, FOLD_CUT, m_high[:, k, :], m_low[:, k, :])
                d = s - 1
                mm(sums[:, 3 * par + d // 3, bass.ds(d % 3 * P, P)], ident_r[:, :], ident_r[:, :])\
                    .then_inc(contracted, 1)

            with pe_loop(FOLDS // 2) as j:
                fold_tile(2 * j + HEAD_TILES, j, 0)
                fold_tile(2 * j + HEAD_TILES + 1, j, 1)
            fold_tile(KC, FOLDS // 2, 0)

            def token_tile(t, j, odd):
                par = TPAR[odd]
                slot = SLOT[par]

                def part(kind, k, p):
                    return product(kind, slot, k, par, p, TOKEN_CUT, c_high[:, 1 + k, :], c_low[:, 1 + k, :])

                def wide_parts(steps):
                    for n in steps:
                        if n == 3 * (KC - 1):
                            pe.wait_ge(read_out[0], FOLD_PIECES[0])
                        for p in (0, 1):
                            last = part(n % 3, n // 3, p)
                    return last

                pe.wait_ge(low_made, t + HEAD_LOADS + FOLDS + 1)
                pe.wait_ge(read_out[par], 3 * j + FOLD_PIECES[par])
                for k in range(KC):
                    if k == KC - 1:
                        pe.wait_ge(read_out[0], FOLD_PIECES[0] - 2)
                    for kind in (HH, HL, LH):
                        last = part(kind, k, 2)
                last.then_inc(narrow_ready, 1)
                wide_parts(range(0, TURN_AT))
                pe.wait_ge(u_ready, t + 1)
                nc.tensor.transpose(ut_psum, u[:, :], ident[:, :]).then_inc(u_turned, 1)
                wide_parts(range(TURN_AT, LORA_AT))
                pe.wait_ge(ut_low_ready, t + 1)
                parts = ((ut_high, c_high), (ut_high, c_low), (ut_low, c_high))
                for lhs, rhs in parts:
                    last = mm(piece(par, 2, 0, MCOLS - 2 * WIDE), lhs[:, :], rhs[:, 0, 2 * WIDE:MCOLS])
                last.then_inc(y_small_ready, 1)
                wide_parts(range(LORA_AT, 3 * KC)).then_inc(contracted, 1)
                pe.wait_ge(v_ready, t + 1)
                nc.tensor.transpose(vt_psum, v_rows[:, :], ident[:, :]).then_inc(v_turned, 1)
                for lhs, rhs in parts:
                    for p in (0, 1):
                        mm(piece(par, p, 0, WIDE), lhs[:, :], rhs[:, 0, p * WIDE:(p + 1) * WIDE])
                pe.wait_ge(vt_ready, t + 1)
                for p, a, b in ((0, 0, WIDE), (2, 2 * WIDE, D), (1, WIDE, 2 * WIDE)):
                    mm(piece(par, p, 0, b - a), vt[:, :], mix[:, a:b]).then_inc(z_ready, 1)

            pe.wait_ge(gate_split, 1)
            pe.wait_ge(mix_split, 1)
            with pe_loop(TILES // 2) as j:
                token_tile(2 * j, j, 0)
                token_tile(2 * j + 1, j, 1)


def kernel(**inputs):
    import numpy as np
    import concourse.bacc as bacc
    from concourse.bass_utils import run_bass_kernel_spmd

    P = 128
    x = np.asarray(inputs["x"])
    batch, seq, D = x.shape
    KC = D // P
    tokens = batch * seq
    tiles = tokens // P
    W, Wr, A, B = (np.asarray(inputs["L0_cond_" + n]) for n in ("W", "Wr", "A", "B"))
    Wf, bf, Af, Bm, Wrf = (np.asarray(inputs["L0_ffn_" + n]) for n in ("W", "b", "A", "Bm", "Wr"))

    m_t = np.concatenate([Wf, Wrf, Af.reshape(-1, D)], axis=0).T
    b_t = B.transpose(1, 0, 2).reshape(D, -1)
    head = np.concatenate([m_t, b_t, W[:, :P]], axis=1).reshape(KC, P, -1)
    fold_tail = W[:, P:].reshape(KC, P, KC - 1, P).transpose(2, 1, 0, 3).reshape(KC - 1, P, D)
    x_t = x.reshape(tiles, P, KC, P).transpose(0, 3, 2, 1).reshape(tiles, P, D)
    gate_proj = np.concatenate([A.reshape(-1, D), Wr], axis=0).T.reshape(KC, P, -1).transpose(1, 0, 2)
    bm_t = Bm.transpose(0, 2, 1).reshape(-1, D)
    mix_rows = np.concatenate([bm_t, bm_t, bm_t, bf[None], bf[None]], axis=0)
    language = np.repeat(np.asarray(inputs["itok_B_0_7"]), seq).reshape(tiles, P).T

    arrays = dict(head=head, fold_tail=fold_tail, tokens=x_t, gate_proj=gate_proj, mix_rows=mix_rows,
                  language=language)
    arrays = {n: np.ascontiguousarray(a) for n, a in arrays.items()}
    nc = bacc.Bacc("TRN2", target_bir_lowering=False, num_devices=1)
    args = [nc.dram_tensor(n, a.shape, mybir.dt.from_np(a.dtype), kind="ExternalInput").ap()
            for n, a in arrays.items()]
    out = nc.dram_tensor("out", (tokens, D), mybir.dt.float32, kind="ExternalOutput").ap()
    adaln_ffn_kernel(nc, *args, out)
    r = run_bass_kernel_spmd(nc, [arrays], core_ids=[0])
    return r.results[0]["out"].reshape(batch, seq, D)
```
